# Optimizing a Trainium2 kernel written in Bass

```python
import numpy as np
import jax
import jax.numpy as jnp

def _softmax(x, axis=-1):
    return jax.nn.softmax(x, axis=axis)

def _gelu(x):
    return jax.nn.gelu(x, approximate=True)

def _silu(x):
    return jax.nn.silu(x)

def _sigmoid(x):
    return jax.nn.sigmoid(x)

def _layernorm(x, axis=-1, eps=1e-05):
    m = jnp.mean(x, axis=axis, keepdims=True)
    v = jnp.var(x, axis=axis, keepdims=True)
    return (x - m) / jnp.sqrt(v + eps)

def _scatter_add(tgt, idx, src, axis=0):
    return tgt.at[idx].add(src)

def _segment_sum(src, seg, n):
    return jax.ops.segment_sum(src, seg, n)
kernel_name = 'mk_decoder_preln_d1_seqx_r4_5e0e0f'

def setup_inputs(seed: int=0):
    np.random.seed(seed)
    _w = jnp.asarray

    def _rec_inputs():
        import jax
        import jax.numpy as jnp
        _rk = jax.random.key(seed)
        x = -0.000125 + 0.9999 * jax.random.normal(jax.random.fold_in(_rk, 1), (4, 512, 512), jnp.float32)
        _lenS = 512 - jax.random.randint(jax.random.fold_in(_rk, 7), (4,), 0, max(1, 512 // 4) + 1, jnp.int32)
        _lenS2 = 512 - jax.random.randint(jax.random.fold_in(_rk, 8), (4,), 0, max(1, 512 // 4) + 1, jnp.int32)
        itok_BxS_13_99985 = jax.random.randint(jax.random.fold_in(_rk, 11), (4, 512), 13, 99986, jnp.int32)
        _ctx_2048P = jax.random.normal(jax.random.fold_in(_rk, 12), (4, 16, 512), jnp.float32)
        _ctx_2048c = jax.random.dirichlet(jax.random.fold_in(_rk, 512), 0.3 * jnp.ones((16,), jnp.float32), (4, 512))
        _ctx_2048t = jnp.einsum('bsk,bkd->bsd', _ctx_2048c, _ctx_2048P)
        _ctx_2048t = _ctx_2048t * jax.lax.rsqrt(jnp.mean(jnp.square(_ctx_2048t)) + 1e-12) * 0.953939
        ctx_2048 = 6.82029e-06 + 0.0200006 * (_ctx_2048t + 0.3 * jax.random.normal(jax.random.fold_in(_rk, 612), (4, 512, 512), jnp.float32))
        return (x, itok_BxS_13_99985, ctx_2048)
    x, itok_BxS_13_99985, ctx_2048 = _rec_inputs()

    def _L0_attn_setup():
        import jax, jax.numpy as jnp
        import numpy as np
        B, L, D = (4, 1024, 512)
        EPS = 1e-05
        W_SCALE = 0.02

        def _hgrn_forward(x, Wi, Wf, Wg, g_norm_weight, Wo):
            i = jnp.einsum('bld,ed->ble', x, Wi)
            f = jnp.einsum('bld,ed->ble', x, Wf)
            gate = jax.nn.sigmoid(f)
            i_in = jax.nn.silu(i) * (1.0 - gate)

            def combine(c1, c2):
                a1, b1 = c1
                a2, b2 = c2
                return (a1 * a2, a2 * b1 + b2)
            _, o = jax.lax.associative_scan(combine, (gate, i_in), axis=1)
            g = jnp.einsum('bld,ed->ble', x, Wg)
            rms = jax.lax.rsqrt(jnp.mean(jnp.square(g), axis=-1, keepdims=True) + EPS)
            out = g * rms * g_norm_weight * (o * jax.nn.sigmoid(o))
            return jnp.einsum('ble,de->bld', out, Wo)
        key = jax.random.key(seed)
        kx, ki, kf, kg, ko = jax.random.split(key, 5)
        return {'hidden_states': jax.random.normal(kx, (B, L, D), dtype=jnp.float32), 'Wi': jax.random.normal(ki, (D, D), dtype=jnp.float32) * W_SCALE, 'Wf': jax.random.normal(kf, (D, D), dtype=jnp.float32) * W_SCALE, 'Wg': jax.random.normal(kg, (D, D), dtype=jnp.float32) * W_SCALE, 'g_norm_weight': jnp.ones((D,), dtype=jnp.float32), 'Wo': jax.random.normal(ko, (D, D), dtype=jnp.float32) * W_SCALE}
    _L0_attn_all = _L0_attn_setup()
    _L0_attn_in = {k: v for k, v in _L0_attn_all.items() if k in ('Wi', 'Wf', 'Wg', 'g_norm_weight', 'Wo')}
    del _L0_attn_all

    def _L0_xattn_setup():
        import jax, jax.numpy as jnp
        import numpy as np
        B, S, D = (4, 1024, 512)
        E = 4
        F = 2048 // E
        VOCAB = 25000
        key = jax.random.key(seed)
        k1, k2, k3, k4, k5 = jax.random.split(key, 5)
        hidden_states = jax.random.normal(k1, (B, S, D), dtype=jnp.float32)
        token_ids = jax.random.randint(k2, (B, S), 0, VOCAB, dtype=jnp.int64)
        Wg = jax.random.normal(k3, (E, F, D), dtype=jnp.float32) * 0.02
        Wu = jax.random.normal(k4, (E, F, D), dtype=jnp.float32) * 0.02
        Wd = jax.random.normal(k5, (E, D, F), dtype=jnp.float32) * 0.02
        return {'hidden_states': hidden_states, 'token_ids': token_ids, 'Wg': Wg, 'Wu': Wu, 'Wd': Wd}
    _L0_xattn_all = _L0_xattn_setup()
    _L0_xattn_in = {k: v for k, v in _L0_xattn_all.items() if k in ()}
    del _L0_xattn_all

    def _L0_ffn_setup():
        import jax, jax.numpy as jnp
        import numpy as np
        NUM_EXPERTS = 8
        HIDDEN = 512
        INTER = 512
        TOP_K = 2
        key = jax.random.key(seed)
        ks = jax.random.split(key, 7)
        hidden_states = jax.random.normal(ks[0], (4, 512, HIDDEN), dtype=jnp.float32)
        gate_w = jax.random.normal(ks[1], (HIDDEN, NUM_EXPERTS), dtype=jnp.float32) * 0.02
        fc1_w = jax.random.normal(ks[2], (NUM_EXPERTS, HIDDEN, INTER), dtype=jnp.float32) * 0.02
        fc1_b = jnp.zeros((NUM_EXPERTS, INTER), dtype=jnp.float32)
        fc2_w = jax.random.normal(ks[3], (NUM_EXPERTS, INTER, HIDDEN), dtype=jnp.float32) * 0.02
        fc2_b = jnp.zeros((NUM_EXPERTS, HIDDEN), dtype=jnp.float32)
        alpha = jax.random.normal(ks[4], (NUM_EXPERTS,), dtype=jnp.float32)
        return {'hidden_states': hidden_states, 'gate_w': gate_w, 'fc1_w': fc1_w, 'fc1_b': fc1_b, 'fc2_w': fc2_w, 'fc2_b': fc2_b, 'alpha': alpha}
    _L0_ffn_all = _L0_ffn_setup()
    _L0_ffn_in = {k: v for k, v in _L0_ffn_all.items() if k in ('gate_w', 'fc1_w', 'fc1_b', 'fc2_w', 'fc2_b', 'alpha')}
    del _L0_ffn_all
    return {'x': x, 'itok_BxS_13_99985': itok_BxS_13_99985, 'ctx_2048': ctx_2048, 'L0_attn_Wi': _L0_attn_in['Wi'], 'L0_attn_Wf': _L0_attn_in['Wf'], 'L0_attn_Wg': _L0_attn_in['Wg'], 'L0_attn_g_norm_weight': _L0_attn_in['g_norm_weight'], 'L0_attn_Wo': _L0_attn_in['Wo'], 'L0_ffn_gate_w': _L0_ffn_in['gate_w'], 'L0_ffn_fc1_w': _L0_ffn_in['fc1_w'], 'L0_ffn_fc1_b': _L0_ffn_in['fc1_b'], 'L0_ffn_fc2_w': _L0_ffn_in['fc2_w'], 'L0_ffn_fc2_b': _L0_ffn_in['fc2_b'], 'L0_ffn_alpha': _L0_ffn_in['alpha']}

def reference(x, itok_BxS_13_99985, ctx_2048, L0_attn_Wi, L0_attn_Wf, L0_attn_Wg, L0_attn_g_norm_weight, L0_attn_Wo, L0_ffn_gate_w, L0_ffn_fc1_w, L0_ffn_fc1_b, L0_ffn_fc2_w, L0_ffn_fc2_b, L0_ffn_alpha):
    import jax
    import jax.numpy as jnp

    def _L0_attn_ref(hidden_states, Wi, Wf, Wg, g_norm_weight, Wo):
        import jax, jax.numpy as jnp
        import numpy as np
        B, L, D = (4, 1024, 512)
        EPS = 1e-05
        W_SCALE = 0.02

        def _hgrn_forward(x, Wi, Wf, Wg, g_norm_weight, Wo):
            i = jnp.einsum('bld,ed->ble', x, Wi)
            f = jnp.einsum('bld,ed->ble', x, Wf)
            gate = jax.nn.sigmoid(f)
            i_in = jax.nn.silu(i) * (1.0 - gate)

            def combine(c1, c2):
                a1, b1 = c1
                a2, b2 = c2
                return (a1 * a2, a2 * b1 + b2)
            _, o = jax.lax.associative_scan(combine, (gate, i_in), axis=1)
            g = jnp.einsum('bld,ed->ble', x, Wg)
            rms = jax.lax.rsqrt(jnp.mean(jnp.square(g), axis=-1, keepdims=True) + EPS)
            out = g * rms * g_norm_weight * (o * jax.nn.sigmoid(o))
            return jnp.einsum('ble,de->bld', out, Wo)
        return _hgrn_forward(hidden_states, Wi, Wf, Wg, g_norm_weight, Wo)

    def _L0_xattn_ref(hidden_states, token_ids, Wg, Wu, Wd):
        import jax, jax.numpy as jnp
        import numpy as np
        B, S, D = (4, 1024, 512)
        E = 4
        F = 2048 // E
        VOCAB = 25000
        tokens_per_expert = VOCAB // E
        tid = jnp.clip(token_ids, 0, VOCAB - 1)
        expert_ids = jnp.minimum(tid // tokens_per_expert, E - 1)
        out = jnp.zeros_like(hidden_states)
        for e in range(E):
            g = jax.nn.silu(jnp.einsum('bsd,fd->bsf', hidden_states, Wg[e]))
            u = jnp.einsum('bsd,fd->bsf', hidden_states, Wu[e])
            y = jnp.einsum('bsf,df->bsd', g * u, Wd[e])
            out = jnp.where((expert_ids == e)[..., None], y, out)
        return out

    def _L0_ffn_ref(hidden_states, gate_w, fc1_w, fc1_b, fc2_w, fc2_b, alpha):
        import jax, jax.numpy as jnp
        import numpy as np
        NUM_EXPERTS = 8
        HIDDEN = 512
        INTER = 512
        TOP_K = 2
        B, S, H = hidden_states.shape
        x = hidden_states.reshape(-1, H)
        probs = jax.nn.softmax(x @ gate_w, axis=-1)
        gate_score, gate_idx = jax.lax.top_k(probs, TOP_K)
        gate_score = gate_score / jnp.sum(gate_score, axis=-1, keepdims=True)
        onehot = jax.nn.one_hot(gate_idx, NUM_EXPERTS, dtype=x.dtype)
        combine = jnp.einsum('tk,tke->te', gate_score, onehot) * alpha[None, :]
        h = jnp.einsum('th,ehi->eti', x, fc1_w) + fc1_b[:, None, :]
        h = jax.nn.gelu(h, approximate=False)
        y = jnp.einsum('eti,eih->eth', h, fc2_w) + fc2_b[:, None, :]
        out = jnp.einsum('eth,te->th', y, combine)
        return out.reshape(B, S, H)
    x = x + _L0_attn_ref(_layernorm(x, axis=-1), L0_attn_Wi, L0_attn_Wf, L0_attn_Wg, L0_attn_g_norm_weight, L0_attn_Wo)
    x = x + _L0_xattn_ref(_layernorm(x, axis=-1), itok_BxS_13_99985, ctx_2048, ctx_2048, ctx_2048)
    x = x + _L0_ffn_ref(_layernorm(x, axis=-1), L0_ffn_gate_w, L0_ffn_fc1_w, L0_ffn_fc1_b, L0_ffn_fc2_w, L0_ffn_fc2_b, L0_ffn_alpha)
    return x

_drawn_inputs = setup_inputs


def setup_inputs(seed=0):
    import zlib

    import numpy as np

    out = dict(_drawn_inputs(seed))
    spreads = {'L0_attn_g_norm_weight': (1.0, 0.6),
     'L0_ffn_fc1_b': (0.0, 0.414),
     'L0_ffn_fc2_b': (0.0, 0.1)}
    factors = {'L0_attn_Wf': 2.782}
    for name, (base, spread) in spreads.items():
        noise = np.random.default_rng([zlib.crc32(name.encode()), seed]).standard_normal(out[name].shape)
        drawn = base * np.exp(spread * noise) if base else spread * noise
        out[name] = jnp.asarray(drawn.astype(out[name].dtype))
    for name, factor in factors.items():
        out[name] = (out[name] * factor).astype(out[name].dtype)
    return out
```

```python
import concourse.bass as bass
from concourse import mybir
from contextlib import ExitStack

P = 128
D = 512
C = D // P
BATCH, SEQ = 4, 512
TOK = BATCH * SEQ
ROWS = TOK + P
TB = SEQ // P
T16 = TOK // P
E2, E3, TOPK = 4, 8, 2
NB2 = (TOK + E2 * (P - 1)) // P
NB3 = (TOK * TOPK + E3 * (P - 1)) // P
PER_EXPERT = 25000 // E2
EPS = 1e-5
FIT = 14
X_SCALE = 16.0


def decoder_layer(nc, x, tid, ctxT, wiT, wfT, wgT, gnorm, woT, gate_w, expert_w, fc1_b, fc2_b, alpha, out):
    f32, f32r, bf16, f16, i32 = (mybir.dt.float32, mybir.dt.float32r, mybir.dt.bfloat16,
                                 mybir.dt.float16, mybir.dt.int32)
    ALU = mybir.AluOpType
    ACT = mybir.ActivationFunctionType
    AX = mybir.AxisListType
    ds = bass.ds

    BASE = 16512
    REG_C, REG_A, REG_B = BASE, BASE + 65536, BASE + 2 * 65536
    REG_D, END = BASE + 3 * 65536, 229344
    top = {}

    def at(region, name, shape, dt):
        size = 4
        for n in shape[1:]:
            size *= n
        if dt in (bf16, f16):
            size //= 2
        off = top.get(region, region[0])
        t = nc.alloc_sbuf_tensor_at(name, shape, dt, offset=off)
        top[region] = off + (size + 31) // 32 * 32
        assert top[region] <= region[1], (name, top[region], region)
        return t

    d = (REG_D, END, "small")
    stage = at(d, "ctx_stage", [P, C, D], f32)
    ident = at(d, "ident", [P, P], f32)
    iota = at(d, "iota_row", [P, P], f32)
    before = at(d, "before", [P, P], bf16)
    ones_b = at(d, "ones_bf16", [P, P], bf16)
    ones = at(d, "ones_column", [P, 1], f32)
    minus_half = at(d, "minus_half", [P, TB], f32)
    spare_row = at(d, "spare_row", [P, 1], f32)
    tok1 = at(d, "token_number", [P, T16], f32)
    gn = at(d, "gnorm_column", [P, C], f32)
    gatew = at(d, "gate_w", [P, C, E3], f32)
    alpha_b = at(d, "alpha_rows", [P, E3], f32)
    tid_i = at(d, "token_class_i", [P, T16], i32)
    tid_f = at(d, "token_class", [P, T16], f32)
    cls = at(d, "expert_of_token", [P, T16], f32)
    zero_n = at(d, "zeros_small", [P, 32], f32)
    mask2 = at(d, "mask2", [P, T16, E2], bf16)
    tot2 = at(d, "tile_totals2", [P, T16, E2], f32)
    cum2 = at(d, "running_totals2", [P, T16, E2], f32)
    rank2 = at(d, "rank2", [P, T16, E2], f32)
    slot2 = at(d, "slot2", [P, 2, T16], f32)
    slot2_i = at(d, "slot2_i", [P, 3, T16], i32)
    cnt = at(d, "counts", [P, E3], f32)
    cnt_i = at(d, "counts_i", [P, E3], i32)
    blocks = at(d, "blocks", [P, E3], f32)
    ends = at(d, "end_blocks", [P, E3], f32)
    firsts = at(d, "first_slots", [P, E3], f32)
    eb_f = at(d, "expert_of_block_f", [P, NB3], f32)
    eb2 = at(d, "expert_of_block2", [P, NB2], i32)
    eb3 = at(d, "expert_of_block3", [P, NB3], i32)
    tokv2 = at(d, "token_of_slot2", [P, NB2], f32)
    pad2 = at(d, "pad2", [P, NB2], f32)
    row2 = at(d, "row_of_slot2", [P, NB2 + 3], i32)
    row3 = at(d, "row_of_slot3", [P, NB3 + 2], i32)
    w3 = at(d, "weight_of_slot3", [P, NB3], f32)
    idx_in = at(d, "rows_to_gather", [P, 4], i32)
    idx_out = at(d, "rows_to_scatter", [P, 4], i32)
    bn = at(d, "bn_stats", [P, TB, 6], f32)
    mv = at(d, "mean_var", [P, TB, 2], f32)
    veps = at(d, "var_eps", [P, TB], f32)
    rstd = at(d, "rstd", [P, TB], f32)
    ms = at(d, "mean_square", [P, TB], f32)
    rms = at(d, "rms", [P, TB], f32)
    bn3 = at(d, "bn_stats3", [P, 6], f32)
    mv3 = at(d, "mean_var3", [P, 2], f32)
    veps3 = at(d, "var_eps3", [P, 1], f32)
    rstd3 = at(d, "rstd3", [P, 1], f32)
    sqs = at(d, "square_sums", [P, 2 * E3 + 1], f32)
    sq_sum = at(d, "square_sum", [P, 3], f32)
    sq_sum_b = at(d, "square_sum_bf16", [P, 4], bf16)
    bounds = at(d, "bounds", [P, 3], f32)
    scale_i = at(d, "scales_i", [P, 3], i32)
    undo_i = at(d, "scales_undone_i", [P, 3], i32)
    wscale = at(d, "scale_of_matrix", [P, 2 * E3], f32)
    undo = at(d, "undo", [P, 2], f32)
    b1t = at(d, "fc1_bias_tile", [P, E3 * D // P], f32)

    c1 = (REG_C, REG_A, "ctx")
    ctxw = at(c1, "ctx_w", [P, E2, 2, C, D], f32r)
    craw = (REG_C + 32768, REG_A, "raw")
    raw = at(craw, "attn_raw", [P, 4, C, D], f32)
    attw = at((REG_A, REG_B, "attn"), "attn_w", [P, 4, 2, C, D], f32r)
    wm = at((REG_A, REG_D, "experts"), "expert_w", [P, 2 * E3, 2, C, D], f16)
    b1 = (REG_B, REG_D, "attn_act")
    xn = at(b1, "x_norm", [P, TB, D], f32)
    xT = at(b1, "x_norm_T", [P, 2, C, SEQ], f32r)
    oT = at(b1, "mixed_T", [P, 2, C, SEQ], f32r)
    xres = at(b1, "x_residual", [P, TB, D], f32)
    gate, keep, sig_i, inp, state, sig_o, gsq, mixed = (
        at(b1, n, [P, SEQ], f32) for n in
        ("gate", "one_minus_gate", "sigmoid_i", "scan_input", "scan_state", "sigmoid_o", "g_squared", "mixed"))
    onehot2 = at(d, "onehot_row2", [P, 4, P], f32)
    onehotb2 = at(d, "onehot_block2", [P, 4, NB2], f32)
    b2 = (REG_B + 32768, REG_D, "ctx_act")
    x1g = at(b2, "x1_rows", [P, 4, D], f32)
    x2n = at(b2, "x1_norm", [P, D], f32)
    x2T = at(b2, "x1_norm_T", [P, 2, C, P], f32r)
    sil = at(b2, "silu_z", [P, D], f32)
    hh = at(b2, "hidden2", [P, D], f32)
    hT = at(b2, "hidden2_T", [P, 2, C, P], f32r)
    x2b = at(b2, "x2_rows", [P, 2, D], f32)
    x3b = at(b2, "x2_norm", [P, 2, D], f32)
    x3T = at(b2, "x2_norm_T", [P, C, P], f32)
    c3 = (REG_C, REG_A, "moe")
    bias1 = at(c3, "fc1_bias_rows", [P, E3, D], f32)
    bias2 = at(c3, "fc2_bias_rows", [P, E3, D], f32)
    xg = at(c3, "x3_rows", [P, 4, D], f32)
    xgT = at(c3, "x3_T", [P, 2, C * P], f16)
    hb = at(c3, "hidden3_pre", [P, D], f32)
    hg = at(c3, "hidden3", [P, D], f32)
    hgT = at(c3, "hidden3_T", [P, 2, C * P], f16)
    yb = at(c3, "y_rows", [P, 2, D], f32)
    lg = at(c3, "logits", [P, NB2, E3], f32)
    pr = at(c3, "probs", [P, NB2, E3], f32)
    t8 = at(c3, "scratch8", [P, NB2, E3], f32)
    m1 = at(c3, "mask_first", [P, NB2, E3], f32)
    m2 = at(c3, "mask_second", [P, NB2, E3], f32)
    mb = at(c3, "mask_both", [P, NB2, E3], bf16)
    tot3 = at(c3, "tile_totals3", [P, NB2, E3], f32)
    cum3 = at(c3, "running_totals3", [P, NB2, E3], f32)
    rank3 = at(c3, "rank3", [P, NB2, E3], f32)
    red = at(c3, "reductions", [P, 8, NB2], f32)
    real = at(c3, "slot_is_real", [P, NB2], f32)
    slot3 = at(c3, "slot3", [P, 2, TOPK, NB2], f32)
    slot3_i = at(c3, "slot3_i", [P, 3, TOPK, NB2], i32)
    onehot3 = at(c3, "onehot_row3", [P, 4, P], f32)
    onehotb3 = at(c3, "onehot_block3", [P, 4, 2, NB3], f32)

    bank = [nc.alloc_psum_tensor(f"bank{n}", [P, 512], f32) for n in range(8)]
    ps_f, ps_i, ps_g, ps_ss = bank[0], bank[1], bank[2], bank[7]
    ps_t, ps_y = (bank[3], bank[4]), (bank[5], bank[6])
    ps_h, ps_o, ps_xt, ps_ht, ps_x3t, ps_lg, ps_route = bank[0], bank[1], bank[2], bank[3], bank[4], bank[5], bank[6]

    x1_rows = nc.dram_tensor("x1_rows_dram", [ROWS, D], f32, kind="Internal").ap()
    x3_rows = nc.dram_tensor("x3_rows_dram", [ROWS, D], f32, kind="Internal").ap()

    ctx = ExitStack()
    with ctx:
        def sem(name):
            return ctx.enter_context(nc.semaphore(name))

        def wait(eng, s, value):
            if not (isinstance(value, int) and value <= 0):
                eng.wait_ge(s, value)

        consts = sem("consts"); filled = sem("filled"); small_in = sem("small_in"); class_in = sem("class_in")
        zeroed = sem("zeroed"); spare_done = sem("spare_done")
        raw_in = [sem(f"raw_in{n}") for n in range(4)]
        raw_hi = sem("raw_hi"); raw_lo = sem("raw_lo")
        ctx_in = sem("ctx_in"); ctx_hi = sem("ctx_hi"); ctx_lo = sem("ctx_lo")
        x_in = sem("x_in"); res_in = sem("res_in"); x1_stored = sem("x1_stored")
        stats1 = sem("stats1"); mean1 = sem("mean1"); var1 = sem("var1"); rstd1 = sem("rstd1"); x_normed = sem("x_normed")
        t_done = sem("t_done"); xT_hi = sem("xT_hi"); xT_lo = sem("xT_lo")
        f_done = sem("f_done"); i_done = sem("i_done"); g_done = sem("g_done"); ss_done = sem("ss_done")
        gate_done = sem("gate_done"); keep_done = sem("keep_done"); sigi_done = sem("sigi_done")
        gsq_done = sem("gsq_done"); sigo_done = sem("sigo_done")
        isig_done = sem("isig_done"); inp_done = sem("inp_done"); state_done = sem("state_done")
        go_done = sem("go_done"); mixed_done = sem("mixed_done"); oT_hi = sem("oT_hi"); oT_lo = sem("oT_lo")
        ms_done = sem("ms_done"); rms_done = sem("rms_done"); y_done = sem("y_done"); x1_done = sem("x1_done")
        chain = sem("route_step")
        mask2_done = sem("mask2_done"); rank2_done = sem("rank2_done")
        eb2_done = sem("eb2_done"); eb3_done = sem("eb3_done")
        hot2 = sem("hot2"); hot2_used = sem("hot2_used"); row2_done = sem("row2_done")
        mask3_done = sem("mask3_done"); rank3_done = sem("rank3_done")
        hot3 = sem("hot3"); hot3_used = sem("hot3_used"); row3_done = sem("row3_done"); w3_done = sem("w3_done")
        lg_ready = sem("lg_ready"); exp_done = sem("exp_done"); max_done = sem("max_done")
        turns = sem("indirect_turns"); idx_set = sem("idx_set"); idx_out_set = sem("idx_out_set")
        x1g_in = [sem(f"x1g_in{n}") for n in range(4)]
        stats2 = sem("stats2"); mean2 = sem("mean2"); var2 = sem("var2"); rstd2 = sem("rstd2"); x2n_done = sem("x2n_done")
        xt2_done = sem("xt2_done"); x2T_hi = sem("x2T_hi"); x2T_lo = sem("x2T_lo")
        z2_done = sem("z2_done"); sil_done = sem("sil_done"); h2_done = sem("h2_done")
        ht2_done = sem("ht2_done"); hT_hi = sem("hT_hi"); hT_lo = sem("hT_lo")
        y2_done = sem("y2_done"); x2_done = sem("x2_done"); stats3 = sem("stats3"); mean3 = sem("mean3")
        var3 = sem("var3"); rstd3_done = sem("rstd3_done"); x3_done = sem("x3_done")
        t3_done = sem("t3_done"); x3T_done = sem("x3T_done"); lg_done = sem("lg_done")
        x2_stored = sem("x2_stored"); x3_stored = sem("x3_stored")
        bias_in = sem("bias_in"); bias_tile_in = sem("bias_tile_in")
        pre_in = [sem(f"pre_in{n}") for n in range(4)]
        measured = sem("measured"); sums_done = sem("sums_done"); sums_spread = sem("sums_spread")
        bounds_done = sem("bounds_done"); roots_done = sem("roots_done"); scales_done = sem("scales_done")
        wraw_in = sem("wraw_in"); w_hi = sem("w_hi"); w_lo = sem("w_lo")
        xg_in = [sem(f"xg_in{n}") for n in range(4)]
        idx3_set = sem("idx3_set"); idx3_out_set = sem("idx3_out_set")
        xt3_done = sem("xt3_done"); xgT_hi = sem("xgT_hi"); xgT_lo = sem("xgT_lo"); z3_done = sem("z3_done"); hb_done = sem("hb_done")
        hg_done = sem("hg_done"); ht3_done = sem("ht3_done"); hgT_hi = sem("hgT_hi"); hgT_lo = sem("hgT_lo"); y3_done = sem("y3_done")
        yb_done = sem("yb_done"); yw_done = sem("yw_done"); added = sem("added")

        def one(ap):
            return ap.rearrange("p a n -> p (a n)")

        def one2(ap):
            return ap.rearrange("p a c n -> p (a c n)")

        def first(b):
            return isinstance(b, int) and b == 0

        h_scale = scale_i[:, 2:3].bitcast(f32)

        block = ctx.enter_context(nc.Block())

        x_v = x.rearrange("(n p) d -> p n d", p=P)
        x1_v = x1_rows.rearrange("(n p) d -> p n d", p=P)

        def weights(w):
            return w.rearrange("(c p) n -> p c n", p=P)

        def matrix(m):
            return weights(expert_w[ds(m * D, D), :])

        @block.sync
        def _(sp):
            sp.dma_start(xn[:, :, :], x_v[:, 0:TB, :]).then_inc(x_in, 16)
            for n, w in enumerate((wfT, wiT, wgT, woT)):
                sp.dma_start(raw[:, n, :, :], weights(w)).then_inc(raw_in[n], 16)
                if n == 0:
                    sp.dma_start(gn[:, :], gnorm).then_inc(small_in, 16)
            sp.dma_start(gatew[:, :, :], gate_w.rearrange("(c p) e -> p c e", p=P)).then_inc(small_in, 16)
            sp.dma_start(alpha_b[:, :], alpha.partition_broadcast(P)).then_inc(small_in, 16)
            sp.dma_start(tid_i[:, :], tid).then_inc(class_in, 16)
            sp.dma_start(b1t[:, :], fc1_b.rearrange("e (a k) -> (e a) k", a=P // E3)).then_inc(bias_tile_in, 16)
            sp.wait_ge(zeroed, 1)
            for rows in (x1_rows, x3_rows, out):
                sp.dma_start(rows[TOK:ROWS, :], stage[:, 0, :]).then_inc(spare_done, 16)
            sp.wait_ge(spare_done, 48)

            def batch(b, last):
                if not first(b):
                    sp.wait_ge(ctx_hi, 4 * b)
                    sp.wait_ge(ctx_lo, 4 * b)
                sp.dma_start(stage[:, :, :], weights(ctxT[ds(b * D, D), :])).then_inc(ctx_in, 16)
                if not last:
                    sp.wait_ge(t_done, C * (b + 1))
                    sp.dma_start(xn[:, :, :], x_v[:, ds((b + 1) * TB, TB), :]).then_inc(x_in, 16)
                if not first(b):
                    stores(b - 1)
                    sp.wait_ge(x1_stored, 16 * TB * b)
                sp.dma_start(xres[:, :, :], x_v[:, ds(b * TB, TB), :]).then_inc(res_in, 16)

            def stores(b):
                for t in range(TB):
                    sp.wait_ge(x1_done, TB * b + t + 1)
                    sp.dma_start(x1_v[:, ds(b * TB + t, 1), :], xres[:, t:t + 1, :]).then_inc(x1_stored, 16)

            batch(0, False)
            with sp.Fori(1, BATCH - 1) as b:
                batch(b, False)
            batch(BATCH - 1, True)
            stores(BATCH - 1)
            sp.wait_ge(ctx_hi, C * E2)
            sp.wait_ge(ctx_lo, C * E2)
            sp.dma_start(stage[:, :, :], matrix(0)).then_inc(wraw_in, 16)
            with sp.Fori(1, 2 * E3) as m:
                sp.wait_ge(w_lo, m)
                sp.dma_start(stage[:, :, :], matrix(m)).then_inc(wraw_in, 16)
            sp.wait_ge(y2_done, NB2)
            sp.dma_start(bias1[:, :, :], fc1_b.partition_broadcast(P)).then_inc(bias_in, 16)
            sp.dma_start(bias2[:, :, :], fc2_b.partition_broadcast(P)).then_inc(bias_in, 16)

        @block.gpsimd
        def _(pool):
            pool.memset(ident[:, :], 0.0).then_inc(filled, 1)
            pool.memset(before[:, :], 1.0).then_inc(filled, 1)
            pool.memset(ones_b[:, :], 1.0).then_inc(filled, 1)
            pool.memset(ones[:, :], 1.0).then_inc(filled, 1)
            pool.memset(minus_half[:, :], -0.5).then_inc(filled, 1)
            pool.memset(zero_n[:, :], 0.0).then_inc(filled, 1)
            pool.memset(stage[:, 0, :], 0.0).then_inc(zeroed, 1)
            pool.iota(iota[:, :], [[1, P]], base=0, channel_multiplier=0,
                      allow_small_or_imprecise_dtypes=True).then_inc(filled, 1)
            pool.iota(spare_row[:, :], [[0, 1]], base=TOK + 1, channel_multiplier=1,
                      allow_small_or_imprecise_dtypes=True).then_inc(filled, 1)
            pool.iota(tok1[:, :], [[P, T16]], base=1, channel_multiplier=1,
                      allow_small_or_imprecise_dtypes=True).then_inc(filled, 1)
            pool.wait_ge(filled, 9)
            pool.affine_select(out=ident[:, :], in_=ident[:, :], compare_op=ALU.not_equal, fill=1.0, base=0,
                               pattern=[[-1, P]], channel_multiplier=1).then_inc(consts, 1)
            pool.affine_select(out=before[:, :], in_=before[:, :], compare_op=ALU.is_ge, fill=0.0, base=-1,
                               pattern=[[1, P]], channel_multiplier=-1).then_inc(consts, 1)

            def root1(b):
                pool.wait_ge(var1, b + 1)
                pool.tensor_tensor(rstd[:, :], veps[:, :], minus_half[:, :], ALU.pow).then_inc(rstd1, 1)

            def root_ms(b):
                pool.wait_ge(ms_done, b + 1)
                pool.tensor_tensor(rms[:, :], ms[:, :], minus_half[:, :], ALU.pow).then_inc(rms_done, 1)

            root1(0)
            root1(1)
            with pool.Fori(1, BATCH - 1) as b:
                root_ms(b - 1)
                root1(b + 1)
            root_ms(BATCH - 2)
            root_ms(BATCH - 1)

            def waited():
                pool.sem_inc(turns, 1)

            def rows(dst, k, table, j, done, count):
                pool.tensor_copy(dst[:, k:k + 1], table[:, ds(j, 1)]).then_inc(done, 1)
                pool.wait_ge(done, count)

            def gather2(j, k):
                wait(pool, x2_done, j - 3)
                rows(idx_in, k, row2, j, idx_set, j + 1)
                waited()
                pool.indirect_dma_start(out=x1g[:, k, :], out_offset=None, in_=x1_rows,
                                        in_offset=bass.IndirectOffsetOnAxis(ap=idx_in[:, k:k + 1], axis=0),
                                        ).then_inc(x1g_in[k], 16)

            def root2(j):
                pool.wait_ge(var2, j + 1)
                pool.tensor_tensor(rstd[:, 0:1], veps[:, 0:1], minus_half[:, 0:1], ALU.pow).then_inc(rstd2, 1)

            def root3(j):
                pool.wait_ge(var3, j + 1)
                pool.tensor_tensor(rstd3[:, :], veps3[:, :], minus_half[:, 0:1], ALU.pow).then_inc(rstd3_done, 1)

            def scatter_x2(j, k):
                rows(idx_out, k, row2, j, idx_out_set, j + 1)
                pool.wait_ge(x2_done, j + 1)
                wait(pool, x2_stored, 16 * j)
                waited()
                pool.indirect_dma_start(out=out, out_offset=bass.IndirectOffsetOnAxis(ap=idx_out[:, k:k + 1], axis=0),
                                        in_=x2b[:, k % 2, :], in_offset=None).then_inc(x2_stored, 16)

            def scatter_x3(j, k):
                pool.wait_ge(x3_done, j + 1)
                wait(pool, x3_stored, 16 * j)
                waited()
                pool.indirect_dma_start(out=x3_rows, out_offset=bass.IndirectOffsetOnAxis(ap=idx_out[:, k:k + 1], axis=0),
                                        in_=x3b[:, k % 2, :], in_offset=None).then_inc(x3_stored, 16)

            pool.wait_ge(row2_done, 1)
            pool.wait_ge(x1_stored, 16 * T16)
            gather2(0, 0)
            gather2(1, 1)
            gather2(2, 2)
            pool.wait_ge(bounds_done, 1)
            pool.tensor_tensor(bounds[:, :], bounds[:, :], minus_half[:, 0:3], ALU.pow).then_inc(roots_done, 1)
            root2(0)
            root2(1)

            def step2(j, k):
                static = isinstance(j, int)
                if not static or j + 2 < NB2:
                    root2(j + 2)
                if not static or 1 <= j <= NB2:
                    root3(j - 1)
                if not static or j + 3 < NB2:
                    gather2(j + 3, (k + 3) % 4)
                if not static or 1 <= j <= NB2:
                    scatter_x2(j - 1, (k - 1) % 4)
                if not static or j >= 2:
                    scatter_x3(j - 2, (k - 2) % 4)

            for j in range(4):
                step2(j, j)
            with pool.Fori(4, 16, 4) as j:
                for k in range(4):
                    step2(j + k, k)
            for j in range(16, NB2 + 2):
                step2(j, j % 4)

            def gather3(j, k):
                wait(pool, xt3_done, j - 3)
                rows(idx_in, k, row3, j, idx3_set, j + 1)
                waited()
                pool.indirect_dma_start(out=xg[:, k, :], out_offset=None, in_=x3_rows,
                                        in_offset=bass.IndirectOffsetOnAxis(ap=idx_in[:, k:k + 1], axis=0),
                                        ).then_inc(xg_in[k], 16)

            def add3(j, k):
                rows(idx_out, k, row3, j, idx3_out_set, j + 1)
                pool.wait_ge(yw_done, j + 1)
                wait(pool, added, 16 * j)
                waited()
                pool.indirect_dma_start(out=out, out_offset=bass.IndirectOffsetOnAxis(ap=idx_out[:, k:k + 1], axis=0),
                                        in_=yb[:, k % 2, :], in_offset=None, compute_op=ALU.add).then_inc(added, 16)

            pool.wait_ge(row3_done, 1)
            pool.wait_ge(x2_stored, 16 * NB2)
            pool.wait_ge(x3_stored, 16 * NB2)
            gather3(0, 0)
            gather3(1, 1)

            def step3(j, k):
                static = isinstance(j, int)
                if not static or j + 2 < NB3:
                    gather3(j + 2, (k + 2) % 4)
                if not static or j >= 1:
                    add3(j - 1, (k - 1) % 4)

            for j in range(4):
                step3(j, j)
            with pool.Fori(4, 36, 4) as j:
                for k in range(4):
                    step3(j + k, k)
            for j in range(36, NB3 + 1):
                step3(j, j % 4)
            pool.wait_ge(added, 16 * NB3)

        @block.tensor
        def _(pe):
            pe.wait_ge(consts, 2)

            def three(dst, lhs_hi, lhs_lo, rhs, n, last):
                pe.matmul(dst, lhs_lo, rhs[0], start=(n == 0), stop=False)
                pe.matmul(dst, lhs_hi, rhs[0], start=False, stop=False)
                return pe.matmul(dst, lhs_hi, rhs[1], start=False, stop=last)

            def project(dst, w, e):
                cols = slice(e * P, e * P + P)
                for c in range(C):
                    last = three(dst[:, :], attw[:, w, 0, c, cols], attw[:, w, 1, c, cols],
                                 (xT[:, 0, c, :], xT[:, 1, c, :]), c, c == C - 1)
                return last

            def square_sums(u, e):
                pe.wait_ge(gsq_done, u + 1)
                for t in range(TB):
                    last = pe.matmul(ps_ss[:, t:t + 1], gsq[:, t * P:(t + 1) * P], ones[:, :],
                                     start=(e == 0 and t == 0), stop=(e == C - 1), skip_group_check=True)
                last.then_inc(ss_done, 1)

            def units(b):
                pe.wait_ge(xT_hi, C * (b + 1))
                pe.wait_ge(xT_lo, C * (b + 1))
                for e in range(C):
                    u = C * b + e
                    if first(b) and e == 0:
                        pe.wait_ge(raw_lo, 1)
                    wait(pe, keep_done, u)
                    wait(pe, gate_done, u)
                    project(ps_f, 0, e).then_inc(f_done, 1)
                    if first(b) and e == 0:
                        pe.wait_ge(raw_lo, 2)
                    wait(pe, isig_done, u)
                    project(ps_i, 1, e).then_inc(i_done, 1)
                    if e > 0:
                        square_sums(u - 1, e - 1)
                    if first(b) and e == 0:
                        pe.wait_ge(raw_lo, 3)
                    wait(pe, gsq_done, u)
                    project(ps_g, 2, e).then_inc(g_done, 1)

            def turn_x(b, c):
                n = C * b + c
                pe.wait_ge(x_normed, TB * (b + 1))
                wait(pe, xT_lo, n - 1)
                wait(pe, xT_hi, n - 1)
                for t in range(TB):
                    last = pe.transpose(ps_t[c % 2][:, t * P:(t + 1) * P], xn[:, t, c * P:(c + 1) * P], ident[:, :])
                last.then_inc(t_done, 1)

            def out_project(b, t):
                n = TB * b + t
                pe.wait_ge(oT_hi, C * (b + 1))
                pe.wait_ge(oT_lo, C * (b + 1))
                if t >= 2:
                    wait(pe, x1_done, n - 1)
                rows = slice(t * P, (t + 1) * P)
                for e in range(C):
                    last = three(ps_y[t % 2][:, :], oT[:, 0, e, rows], oT[:, 1, e, rows],
                                 (attw[:, 3, 0, e, :], attw[:, 3, 1, e, :]), e, e == C - 1)
                last.then_inc(y_done, 1)

            def between(b):
                turn_x(b, 0)
                square_sums(C * b - 1, C - 1)
                turn_x(b, 1)
                out_project(b - 1, 0)
                turn_x(b, 2)
                out_project(b - 1, 1)
                turn_x(b, 3)
                out_project(b - 1, 2)
                out_project(b - 1, 3)

            for c in range(C):
                turn_x(0, c)
            units(0)
            pe.wait_ge(raw_lo, 4)
            with pe.Fori(1, BATCH) as b:
                between(b)
                pe.wait_ge(ms_done, b)
                units(b)
            square_sums(C * BATCH - 1, C - 1)
            for t in range(TB):
                out_project(BATCH - 1, t)

            def ranks(masks, n, done):
                pe.matmul(ps_route[:, 0:n], before[:, :], masks, start=True, stop=True)
                pe.matmul(ps_route[:, n:2 * n], ones_b[:, :], masks, start=True, stop=True).then_inc(done, 1)

            pe.wait_ge(mask2_done, 1)
            wait(pe, x1_done, T16 - 0)
            ranks(mask2[:, :, :].rearrange("p t e -> p (t e)"), T16 * E2, rank2_done)
            for t in range(T16):
                pe.wait_ge(hot2, t + 1)
                pe.matmul(ps_route[:, 0:NB2], onehot2[:, t % 4, :], onehotb2[:, t % 4, :],
                          start=(t == 0), stop=(t == T16 - 1)).then_inc(hot2_used, 1)

            pe.wait_ge(sums_done, 1)
            pe.matmul(ps_route[:, 256:259], ones_b[:, :], sq_sum_b[:, 0:3], start=True, stop=True).then_inc(sums_spread, 1)

            pe.wait_ge(ctx_lo, 4 * E2)
            pe.wait_ge(ctx_hi, 4 * E2)

            def expert2(dst, left, e):
                for c in range(C):
                    last = three(dst[:, :], left[:, 0, c, :], left[:, 1, c, :],
                                 (one(ctxw[:, ds(e, 1), 0, c, :]), one(ctxw[:, ds(e, 1), 1, c, :])), c, c == C - 1)
                return last

            def expert_of(table, table_done, j, n):
                pe.wait_ge(table_done, 1)
                return pe.value_load(table[0:1, ds(j, 1)], min_val=0, max_val=n - 1)

            def turn4(dst, src, done):
                for c in range(C):
                    last = pe.transpose(dst[:, c * P:(c + 1) * P], src[:, c * P:(c + 1) * P], ident[:, :])
                last.then_inc(done, 1)

            def turn_in2(j):
                pe.wait_ge(x2n_done, j + 1)
                wait(pe, x2T_lo, j)
                wait(pe, x2T_hi, j)
                turn4(ps_xt, x2n, xt2_done)

            def step2(j, k):
                static = isinstance(j, int)
                if not static or j < NB2:
                    exp_in = expert_of(eb2, eb2_done, j, E2)
                    pe.wait_ge(x2T_lo, j + 1)
                    pe.wait_ge(x2T_hi, j + 1)
                    wait(pe, h2_done, j)
                    expert2(ps_h, x2T, exp_in).then_inc(z2_done, 1)
                if not static or j + 1 < NB2:
                    turn_in2(j + 1)
                if not static or 3 <= j:
                    pe.wait_ge(x3T_done, j - 2)
                    for c in range(C):
                        last = pe.matmul(ps_lg[:, ds((j - 3) * E3, E3)], x3T[:, c, :], gatew[:, c, :],
                                         start=(c == 0), stop=(c == C - 1))
                    last.then_inc(lg_done, 1)
                if not static or 1 <= j <= NB2:
                    exp_out = expert_of(eb2, eb2_done, j - 1, E2)
                    pe.wait_ge(hT_lo, j)
                    pe.wait_ge(hT_hi, j)
                    wait(pe, x2_done, j - 1)
                    expert2(ps_o, hT, exp_out).then_inc(y2_done, 1)
                if not static or j < NB2:
                    pe.wait_ge(h2_done, j + 1)
                    wait(pe, hT_lo, j)
                    wait(pe, hT_hi, j)
                    turn4(ps_ht, hh, ht2_done)
                if not static or 2 <= j < NB2 + 2:
                    pe.wait_ge(x3_done, j - 1)
                    wait(pe, x3T_done, j - 2)
                    turn4(ps_x3t, x3b[:, k % 2, :], t3_done)

            turn_in2(0)
            for j in range(4):
                step2(j, j)
            with pe.Fori(4, 16, 4) as j:
                for k in range(4):
                    step2(j + k, k)
            for j in range(16, NB2 + 3):
                step2(j, j % 4)

            pe.wait_ge(mask3_done, 1)
            n3 = NB2 * E3
            ranks(mb[:, :, :].rearrange("p t e -> p (t e)"), n3, rank3_done)
            for t in range(TOPK * NB2):
                pe.wait_ge(hot3, t + 1)
                pe.matmul(ps_route[:, 0:2 * NB3], onehot3[:, t % 4, :],
                          onehotb3[:, t % 4, :, :].rearrange("p a b -> p (a b)"),
                          start=(t == 0), stop=(t == TOPK * NB2 - 1)).then_inc(hot3_used, 1)

            def expert3(dst, left, first_matrix, e):
                for c in range(C):
                    last = three(dst[:, :], left[:, 0, c * P:(c + 1) * P], left[:, 1, c * P:(c + 1) * P],
                                 (one(wm[:, ds(e + first_matrix, 1), 0, c, :]),
                                  one(wm[:, ds(e + first_matrix, 1), 1, c, :])), c, c == C - 1)
                return last

            def turn_in3(j):
                if isinstance(j, int):
                    pe.wait_ge(xg_in[j % 4], 16 * (j // 4 + 1))
                    src = xg[:, j % 4, :]
                wait(pe, xgT_lo, j)
                turn4(ps_xt, src, xt3_done)

            def step3(j, k):
                static = isinstance(j, int)
                if not static or j < NB3:
                    exp_in = expert_of(eb3, eb3_done, j, E3)
                    pe.wait_ge(xgT_lo, j + 1)
                    wait(pe, hb_done, j)
                    if static and j == 0:
                        pe.wait_ge(w_lo, E3)
                    expert3(ps_h, xgT, 0, exp_in).then_inc(z3_done, 1)
                if not static or j + 1 < NB3:
                    kk = (k + 1) % 4
                    pe.wait_ge(xg_in[kk], 16 * ((j + 1) // 4 + 1) if static else 4 * (j + 1 - kk) + 16)
                    wait(pe, xgT_lo, j + 1)
                    turn4(ps_xt, xg[:, kk, :], xt3_done)
                if not static or 1 <= j:
                    exp_out = expert_of(eb3, eb3_done, j - 1, E3)
                    pe.wait_ge(hgT_lo, j)
                    wait(pe, yb_done, j - 1)
                    if static and j == 1:
                        pe.wait_ge(w_lo, 2 * E3)
                    expert3(ps_o, hgT, E3, exp_out).then_inc(y3_done, 1)
                if not static or j < NB3:
                    pe.wait_ge(hg_done, j + 1)
                    wait(pe, hgT_lo, j)
                    turn4(ps_ht, hg, ht3_done)

            turn_in3(0)
            for j in range(4):
                step3(j, j)
            with pe.Fori(4, 36, 4) as j:
                for k in range(4):
                    step3(j + k, k)
            for j in range(36, NB3 + 1):
                step3(j, j % 4)

        @block.scalar
        def _(act):
            for n in range(4):
                act.wait_ge(raw_in[n], 16)
                act.activation(attw[:, n, 0, :, :], raw[:, n, :, :], ACT.Copy).then_inc(raw_hi, 1)
                if n == 0:
                    for c in range(C):
                        act.wait_ge(t_done, c + 1)
                        act.activation(xT[:, 0, c, :], ps_t[c % 2][:, :], ACT.Copy).then_inc(xT_hi, 1)

            def load_matrix(m):
                act.dma_start(raw[:, m % 4, :, :], matrix(m)).then_inc(pre_in[m % 4], 16)

            def measure(m):
                act.wait_ge(pre_in[m % 4], 16 * (m // 4 + 1))
                act.activation(raw[:, m % 4, :, :], raw[:, m % 4, :, :], ACT.Square,
                               accum_out=sqs[:, m:m + 1]).then_inc(measured, 1)
                if m + 4 < 2 * E3:
                    act.wait_ge(measured, m + 1)
                    load_matrix(m + 4)

            def units(b):
                for e in range(C):
                    u = C * b + e
                    act.wait_ge(f_done, u + 1)
                    wait(act, state_done, u)
                    act.activation(gate[:, :], ps_f[:, :], ACT.Sigmoid).then_inc(gate_done, 1)
                    wait(act, inp_done, u)
                    act.activation(keep[:, :], ps_f[:, :], ACT.Sigmoid, scale=-1.0).then_inc(keep_done, 1)
                    if e == 0:
                        act.wait_ge(ctx_in, 16 * (b + 1))
                    act.wait_ge(i_done, u + 1)
                    wait(act, isig_done, u)
                    act.activation(sig_i[:, :], ps_i[:, :], ACT.Sigmoid).then_inc(sigi_done, 1)
                    act.activation(one(ctxw[:, ds(b, 1), 0, e, :]), stage[:, e, :], ACT.Copy).then_inc(ctx_hi, 1)
                    act.wait_ge(state_done, u + 1)
                    wait(act, go_done, u)
                    act.activation(sig_o[:, :], state[:, :], ACT.Sigmoid).then_inc(sigo_done, 1)
                    act.wait_ge(mixed_done, u + 1)
                    wait(act, y_done, TB * b)
                    act.activation(oT[:, 0, e, :], mixed[:, :], ACT.Copy).then_inc(oT_hi, 1)
                    wait(act, ss_done, u)
                    act.activation(gsq[:, :], ps_g[:, :], ACT.Square).then_inc(gsq_done, 1)
                    if first(b) and e == 0:
                        act.wait_ge(raw_lo, 4)
                        for m in range(4):
                            load_matrix(m)
                    if isinstance(b, int):
                        measure(2 * u)
                        measure(2 * u + 1)

            def between(b):
                for c in range(C):
                    act.wait_ge(t_done, C * b + c + 1)
                    act.wait_ge(g_done, C * b)
                    act.activation(xT[:, 0, c, :], ps_t[c % 2][:, :], ACT.Copy).then_inc(xT_hi, 1)

            units(0)
            between(1)
            units(1)
            act.wait_ge(bias_tile_in, 16)
            act.activation(b1t[:, :], b1t[:, :], ACT.Square, accum_out=sqs[:, 2 * E3:2 * E3 + 1]).then_inc(measured, 1)
            with act.Fori(2, BATCH) as b:
                between(b)
                units(b)

            def step2(j, split):
                static = isinstance(j, int)
                if not static or j < NB2:
                    act.wait_ge(z2_done, j + 1)
                    wait(act, h2_done, j)
                    act.activation(sil[:, :], ps_h[:, :], ACT.Silu).then_inc(sil_done, 1)
                if not static or j + 1 < NB2:
                    turn_in2(j + 1)
                if split is not None:
                    act.wait_ge(wraw_in, 16 * (split + 1))
                    act.wait_ge(scales_done, 1)
                    act.activation(one2(wm[:, ds(split, 1), 0, :, :]), stage[:, :, :].rearrange("p c n -> p (c n)"),
                                   ACT.Copy, scale=wscale[:, ds(split, 1)]).then_inc(w_hi, 1)
                if not static or j < NB2:
                    act.wait_ge(ht2_done, j + 1)
                    wait(act, y2_done, j)
                    act.activation(hT[:, 0, :, :].rearrange("p c q -> p (c q)"), ps_ht[:, :], ACT.Copy).then_inc(hT_hi, 1)
                if not static or j >= 2:
                    act.wait_ge(t3_done, j - 1)
                    wait(act, lg_done, j - 2)
                    act.activation(x3T[:, :, :].rearrange("p c q -> p (c q)"), ps_x3t[:, :], ACT.Copy).then_inc(x3T_done, 1)

            def turn_in2(j):
                act.wait_ge(xt2_done, j + 1)
                wait(act, z2_done, j)
                act.activation(x2T[:, 0, :, :].rearrange("p c q -> p (c q)"), ps_xt[:, :], ACT.Copy).then_inc(x2T_hi, 1)

            turn_in2(0)
            for j in range(4):
                step2(j, None)
            with act.Fori(4, 16) as j:
                step2(j, j - 4)
            for j in range(16, NB2 + 2):
                step2(j, None)

            act.wait_ge(lg_ready, 1)
            act.activation(pr[:, :, :], t8[:, :, :], ACT.Exp).then_inc(exp_done, 1)

            act.wait_ge(x2_stored, 16 * NB2)
            act.wait_ge(x3_stored, 16 * NB2)
            act.wait_ge(lg_done, NB2)
            for m in range(12, 2 * E3):
                act.wait_ge(wraw_in, 16 * (m + 1))
                act.activation(wm[:, m, 0, :, :], stage[:, :, :], ACT.Copy, scale=wscale[:, m:m + 1]).then_inc(w_hi, 1)

            def turn_in3(j):
                act.wait_ge(xt3_done, j + 1)
                wait(act, z3_done, j)
                act.activation(xgT[:, 0, :], ps_xt[:, :], ACT.Copy, scale=X_SCALE).then_inc(xgT_hi, 1)

            def step3(j):
                static = isinstance(j, int)
                if not static or j < NB3:
                    act.wait_ge(hb_done, j + 1)
                    wait(act, ht3_done, j)
                    act.activation(hg[:, :], hb[:, :], ACT.Gelu).then_inc(hg_done, 1)
                if not static or j + 1 < NB3:
                    turn_in3(j + 1)
                if not static or j < NB3:
                    act.wait_ge(ht3_done, j + 1)
                    wait(act, y3_done, j)
                    act.activation(hgT[:, 0, :], ps_ht[:, :], ACT.Copy, scale=h_scale).then_inc(hgT_hi, 1)

            turn_in3(0)
            step3(0)
            with act.Fori(1, NB3 - 1) as j:
                step3(j)
            step3(NB3 - 1)

        @block.vector
        def _(dve):
            steps = [0]

            def link(ins):
                steps[0] += 1
                ins.then_inc(chain, 1)
                dve.wait_ge(chain, steps[0])

            def stats(b):
                for t in range(TB):
                    dve.bn_stats(bn[:, t, :], xn[:, t, :]).then_inc(stats1, 1)

            def means():
                for t in range(TB):
                    dve.bn_aggr(mv[:, t, :], bn[:, t, :]).then_inc(mean1, 1)

            def add_eps(b):
                dve.wait_ge(mean1, TB * (b + 1))
                dve.tensor_scalar(veps[:, :], mv[:, :, 1], EPS, None, ALU.add).then_inc(var1, 1)

            def norm(b):
                dve.wait_ge(rstd1, b + 1)
                for t in range(TB):
                    dve.tensor_scalar(xn[:, t, :], xn[:, t, :], mv[:, t, 0:1], rstd[:, t:t + 1],
                                      ALU.subtract, ALU.mult).then_inc(x_normed, 1)

            def low_x(b, c):
                dve.wait_ge(xT_hi, C * b + c + 1)
                dve.tensor_tensor(xT[:, 1, c, :], ps_t[c % 2][:, :], xT[:, 0, c, :].bitcast(f32),
                                  ALU.subtract).then_inc(xT_lo, 1)

            def low_raw(n):
                dve.wait_ge(raw_hi, n + 1)
                dve.tensor_tensor(attw[:, n, 1, :, :], raw[:, n, :, :], attw[:, n, 0, :, :].bitcast(f32),
                                  ALU.subtract).then_inc(raw_lo, 1)

            def units(b, last):
                for e in range(C):
                    u = C * b + e
                    dve.wait_ge(sigi_done, u + 1)
                    dve.tensor_tensor(inp[:, :], ps_i[:, :], sig_i[:, :], ALU.mult).then_inc(isig_done, 1)
                    dve.wait_ge(isig_done, u + 1)
                    if e == 1 and not last:
                        dve.wait_ge(stats1, TB * (b + 2))
                    dve.wait_ge(keep_done, u + 1)
                    dve.tensor_tensor(inp[:, :], inp[:, :], keep[:, :], ALU.mult).then_inc(inp_done, 1)
                    if e == 1 and not last:
                        means()
                    dve.wait_ge(inp_done, u + 1)
                    dve.wait_ge(gate_done, u + 1)
                    wait(dve, sigo_done, u)
                    wait(dve, go_done, u)
                    dve.tensor_tensor_scan(state[:, :], gate[:, :], inp[:, :], 0.0, ALU.mult, ALU.add).then_inc(state_done, 1)
                    dve.wait_ge(ctx_hi, u + 1)
                    dve.tensor_tensor(one(ctxw[:, ds(b, 1), 1, e, :]), stage[:, e, :],
                                      one(ctxw[:, ds(b, 1), 0, e, :]).bitcast(f32), ALU.subtract).then_inc(ctx_lo, 1)
                    dve.wait_ge(sigo_done, u + 1)
                    dve.scalar_tensor_tensor(state[:, :], state[:, :], gn[:, e:e + 1], sig_o[:, :],
                                             ALU.mult, ALU.mult).then_inc(go_done, 1)
                    dve.wait_ge(go_done, u + 1)
                    dve.wait_ge(g_done, u + 1)
                    wait(dve, oT_lo, u)
                    wait(dve, oT_hi, u)
                    dve.tensor_tensor(mixed[:, :], ps_g[:, :], state[:, :], ALU.mult).then_inc(mixed_done, 1)
                    dve.wait_ge(oT_hi, u + 1)
                    dve.tensor_tensor(oT[:, 1, e, :], mixed[:, :], oT[:, 0, e, :].bitcast(f32),
                                      ALU.subtract).then_inc(oT_lo, 1)
                    if not last:
                        if e == 0:
                            dve.wait_ge(x_in, 16 * (b + 2))
                            stats(b + 1)
                        if e == 1:
                            add_eps(b + 1)
                        if e == 2:
                            norm(b + 1)

            def mean_square(b):
                dve.wait_ge(ss_done, C * (b + 1))
                dve.tensor_scalar(ms[:, :], ps_ss[:, 0:TB], 1.0 / D, EPS, ALU.mult, ALU.add).then_inc(ms_done, 1)

            def residual(b, t):
                n = TB * b + t
                dve.wait_ge(y_done, n + 1)
                dve.wait_ge(rms_done, b + 1)
                if t == 0:
                    dve.wait_ge(res_in, 16 * (b + 1))
                dve.scalar_tensor_tensor(xres[:, t, :], ps_y[t % 2][:, :], rms[:, t:t + 1], xres[:, t, :],
                                         ALU.mult, ALU.add).then_inc(x1_done, 1)

            def between(b):
                low_x(b, 0)
                mean_square(b - 1)
                low_x(b, 1)
                residual(b - 1, 0)
                low_x(b, 2)
                residual(b - 1, 1)
                low_x(b, 3)
                residual(b - 1, 2)
                residual(b - 1, 3)

            dve.wait_ge(x_in, 16)
            dve.wait_ge(filled, 9)
            stats(0)
            dve.wait_ge(stats1, TB)
            means()
            add_eps(0)
            norm(0)
            low_raw(0)
            for c in range(C):
                low_x(0, c)
            for n in (1, 2, 3):
                low_raw(n)
            dve.wait_ge(small_in, 48)

            dve.wait_ge(class_in, 16)
            link(dve.tensor_copy(tid_f[:, :], tid_i[:, :]))
            link(dve.tensor_scalar(cls[:, :], tid_f[:, :], float(PER_EXPERT), None, ALU.is_ge))
            for e in range(2, E2):
                link(dve.scalar_tensor_tensor(cls[:, :], tid_f[:, :], float(PER_EXPERT * e), cls[:, :], ALU.is_ge, ALU.add))
            for e in range(E2):
                last = dve.tensor_scalar(mask2[:, :, e], cls[:, :], float(e), None, ALU.is_equal)
            last.then_inc(mask2_done, 1)

            units(0, False)
            with dve.Fori(1, BATCH - 1) as b:
                between(b)
                units(b, False)
            between(BATCH - 1)
            units(BATCH - 1, True)
            mean_square(BATCH - 1)
            for t in range(TB):
                residual(BATCH - 1, t)

            def place(n_exp, tiles, tot, cum, rank, n_blocks, eb, eb_done):
                n = tiles * n_exp
                link(dve.tensor_copy(tot[:, :, :].rearrange("p t e -> p (t e)"), ps_route[:, n:2 * n]))
                for e in range(n_exp):
                    scan = dve.tensor_tensor_scan(cum[:, :, e], tot[:, :, e], zero_n[:, 0:tiles], 0.0, ALU.add, ALU.add)
                link(scan)
                link(dve.tensor_scalar(cnt[:, 0:n_exp], cum[:, tiles - 1, :], float(P - 1), None, ALU.add))
                link(dve.tensor_copy(cnt_i[:, 0:n_exp], cnt[:, 0:n_exp]))
                link(dve.tensor_scalar(cnt_i[:, 0:n_exp], cnt_i[:, 0:n_exp], 7, None, ALU.arith_shift_right))
                link(dve.tensor_copy(blocks[:, 0:n_exp], cnt_i[:, 0:n_exp]))
                link(dve.tensor_tensor_scan(ends[:, 0:n_exp], blocks[:, 0:n_exp], zero_n[:, 0:n_exp], 0.0, ALU.add, ALU.add))
                link(dve.tensor_tensor(firsts[:, 0:n_exp], ends[:, 0:n_exp], blocks[:, 0:n_exp], ALU.subtract))
                link(dve.tensor_scalar(firsts[:, 0:n_exp], firsts[:, 0:n_exp], float(P), None, ALU.mult))
                flat = "p t e -> p (t e)"
                link(dve.tensor_tensor(cum[:, :, :].rearrange(flat), cum[:, :, :].rearrange(flat),
                                       tot[:, :, :].rearrange(flat), ALU.subtract))
                link(dve.tensor_tensor(rank[:, :, :].rearrange(flat), ps_route[:, 0:n],
                                       cum[:, :, :].rearrange(flat), ALU.add))
                link(dve.tensor_tensor(rank[:, :, :], rank[:, :, :],
                                       firsts[:, 0:n_exp].unsqueeze(1).broadcast_to([P, tiles, n_exp]), ALU.add))
                link(dve.tensor_scalar(eb_f[:, 0:n_blocks], iota[:, 0:n_blocks], ends[:, 0:1], None, ALU.is_ge))
                for e in range(1, n_exp - 1):
                    link(dve.scalar_tensor_tensor(eb_f[:, 0:n_blocks], iota[:, 0:n_blocks], ends[:, e:e + 1],
                                                  eb_f[:, 0:n_blocks], ALU.is_ge, ALU.add))
                dve.tensor_copy(eb[:, :], eb_f[:, 0:n_blocks]).then_inc(eb_done, 1)

            dve.wait_ge(rank2_done, 1)
            place(E2, T16, tot2, cum2, rank2, NB2, eb2, eb2_done)
            link(dve.tensor_tensor(rank2[:, :, :], rank2[:, :, :], mask2[:, :, :], ALU.mult))
            link(dve.tensor_reduce(slot2[:, 0, :], rank2[:, :, :], AX.X, ALU.add))
            link(dve.tensor_copy(slot2_i[:, 0, :], slot2[:, 0, :]))
            link(dve.tensor_scalar(slot2_i[:, 1, :], slot2_i[:, 0, :], P - 1, None, ALU.bitwise_and))
            link(dve.tensor_scalar(slot2_i[:, 2, :], slot2_i[:, 0, :], 7, None, ALU.arith_shift_right))
            link(dve.tensor_copy(slot2[:, :, :], slot2_i[:, 1:3, :]))
            for t in range(T16):
                wait(dve, hot2_used, t - 3)
                dve.tensor_scalar(onehot2[:, t % 4, :], iota[:, :], slot2[:, 0, t:t + 1], None, ALU.is_equal)
                dve.tensor_scalar(onehotb2[:, t % 4, :], iota[:, 0:NB2], slot2[:, 1, t:t + 1], tok1[:, t:t + 1],
                                  ALU.is_equal, ALU.mult).then_inc(hot2, 1)
            dve.wait_ge(hot2_used, T16)
            link(dve.tensor_copy(tokv2[:, :], ps_route[:, 0:NB2]))

            def rows_of(tokv, row, pad, n):
                link(dve.tensor_scalar(pad[:, 0:n], tokv, 0.0, spare_row[:, 0:1], ALU.is_equal, ALU.mult))
                return dve.scalar_tensor_tensor(row, tokv, -1.0, pad[:, 0:n], ALU.add, ALU.add)

            rows_of(tokv2[:, :], row2[:, 0:NB2], pad2, NB2).then_inc(row2_done, 1)

            dve.wait_ge(measured, 2 * E3 + 1)
            for n in range(2):
                last = dve.tensor_reduce(sq_sum[:, n:n + 1], sqs[:, n * E3:(n + 1) * E3], AX.X, ALU.add)
            link(last)
            link(dve.tensor_copy(sq_sum[:, 2:3], sqs[:, 2 * E3:2 * E3 + 1]))
            dve.tensor_copy(sq_sum_b[:, 0:3], sq_sum[:, :]).then_inc(sums_done, 1)
            dve.wait_ge(sums_spread, 1)
            link(dve.tensor_scalar(bounds[:, :], ps_route[:, 256:259], 1e-30, None, ALU.add))
            link(dve.tensor_scalar(bounds[:, 2:3], bounds[:, 2:3], 2.0, None, ALU.mult))
            dve.scalar_tensor_tensor(bounds[:, 2:3], bounds[:, 0:1], 2.0 * D, bounds[:, 2:3],
                                     ALU.mult, ALU.add).then_inc(bounds_done, 1)
            dve.wait_ge(roots_done, 1)
            link(dve.tensor_scalar(bounds[:, :], bounds[:, :], 2.0 ** FIT, None, ALU.mult))
            link(dve.tensor_scalar(scale_i[:, :], bounds[:, :].bitcast(i32), 0x7F800000, None, ALU.bitwise_and))
            link(dve.tensor_scalar(undo_i[:, :], scale_i[:, :], -1.0, float(0x7F000000), ALU.mult, ALU.add))
            link(dve.tensor_scalar(undo[:, 0:1], undo_i[:, 0:1].bitcast(f32), 1.0 / X_SCALE, None, ALU.mult))
            link(dve.tensor_tensor(undo[:, 1:2], undo_i[:, 1:2].bitcast(f32), undo_i[:, 2:3].bitcast(f32), ALU.mult))
            for n in range(2):
                last = dve.tensor_scalar(wscale[:, n * E3:(n + 1) * E3], zero_n[:, 0:E3],
                                         scale_i[:, n:n + 1].bitcast(f32), None, ALU.add)
            last.then_inc(scales_done, 1)

            def x1_stats(j, k):
                dve.wait_ge(x1g_in[k], 4 * (j - k) + 16)
                dve.bn_stats(bn[:, 0, :], x1g[:, k, :]).then_inc(stats2, 1)

            def x1_mean():
                dve.bn_aggr(mv[:, 0, :], bn[:, 0, :]).then_inc(mean2, 1)

            def x1_var(j):
                wait(dve, rstd2, j)
                dve.wait_ge(mean2, j + 1)
                dve.tensor_scalar(veps[:, 0:1], mv[:, 0, 1:2], EPS, None, ALU.add).then_inc(var2, 1)

            def x1_norm(j, k):
                dve.wait_ge(rstd2, j + 1)
                wait(dve, xt2_done, j)
                dve.tensor_scalar(x2n[:, :], x1g[:, k, :], mv[:, 0, 0:1], rstd[:, 0:1],
                                  ALU.subtract, ALU.mult).then_inc(x2n_done, 1)

            def low_x2(j):
                dve.wait_ge(x2T_hi, j + 1)
                flat = "p c q -> p (c q)"
                dve.tensor_tensor(x2T[:, 1, :, :].rearrange(flat), ps_xt[:, :],
                                  x2T[:, 0, :, :].bitcast(f32).rearrange(flat), ALU.subtract).then_inc(x2T_lo, 1)

            def low_weights(m):
                dve.wait_ge(w_hi, m + 1)
                dve.scalar_tensor_tensor(one2(wm[:, ds(m, 1), 1, :, :]), stage[:, :, :].rearrange("p c n -> p (c n)"),
                                         wscale[:, ds(m, 1)], one2(wm[:, ds(m, 1), 0, :, :]),
                                         ALU.mult, ALU.subtract).then_inc(w_lo, 1)

            def step2(j, k, split=None):
                static = isinstance(j, int)
                k1, k2 = (k + 2) % 4, (k - 1) % 4
                kk = k2 % 2
                flat = "p c q -> p (c q)"
                if not static or j < NB2:
                    dve.wait_ge(sil_done, j + 1)
                    wait(dve, ht2_done, j)
                    dve.tensor_tensor(hh[:, :], ps_h[:, :], sil[:, :], ALU.mult).then_inc(h2_done, 1)
                if not static or j + 1 < NB2:
                    low_x2(j + 1)
                ahead = not static or j + 2 < NB2
                if ahead:
                    x1_stats(j + 2, k1)
                if not static or 2 <= j:
                    dve.wait_ge(rstd3_done, j - 1)
                    wait(dve, x3_stored, 16 * (j - 3) if not static or j > 3 else 0)
                    wait(dve, t3_done, j - 3)
                    dve.tensor_scalar(x3b[:, k % 2, :], x2b[:, k % 2, :], mv3[:, 0:1], rstd3[:, 0:1],
                                      ALU.subtract, ALU.mult).then_inc(x3_done, 1)
                if split is not None:
                    low_weights(split)
                if not static or 1 <= j <= NB2:
                    dve.wait_ge(y2_done, j)
                    wait(dve, x2_stored, 16 * (j - 2) if not static or j > 2 else 0)
                    if ahead:
                        dve.wait_ge(stats2, j + 3)
                    dve.tensor_tensor(x2b[:, kk, :], ps_o[:, :], x1g[:, k2, :], ALU.add).then_inc(x2_done, 1)
                    if ahead:
                        x1_mean()
                    dve.wait_ge(x2_done, j)
                    dve.bn_stats(bn3[:, :], x2b[:, kk, :]).then_inc(stats3, 1)
                    dve.wait_ge(stats3, j)
                    wait(dve, x3_done, j - 1)
                    if ahead:
                        x1_var(j + 2)
                    dve.bn_aggr(mv3[:, :], bn3[:, :]).then_inc(mean3, 1)
                    dve.wait_ge(mean3, j)
                    dve.tensor_scalar(veps3[:, :], mv3[:, 1:2], EPS, None, ALU.add).then_inc(var3, 1)
                elif ahead:
                    dve.wait_ge(stats2, j + 3)
                    x1_mean()
                    x1_var(j + 2)
                if not static or j < NB2:
                    dve.wait_ge(hT_hi, j + 1)
                    dve.tensor_tensor(hT[:, 1, :, :].rearrange(flat), ps_ht[:, :],
                                      hT[:, 0, :, :].bitcast(f32).rearrange(flat), ALU.subtract).then_inc(hT_lo, 1)
                if ahead:
                    x1_norm(j + 2, k1)

            for j in range(2):
                x1_stats(j, j)
                dve.wait_ge(stats2, j + 1)
                x1_mean()
                x1_var(j)
                if j == 1:
                    low_x2(0)
                x1_norm(j, j)
            for j in range(4):
                step2(j, j)
            with dve.Fori(4, 16, 4) as j:
                for k in range(4):
                    step2(j + k, k, j + k - 4)
            for j in range(16, NB2 + 2):
                step2(j, j % 4)

            f3 = "p t e -> p (t e)"

            def wide(v):
                return v.unsqueeze(2).broadcast_to([P, NB2, E3])

            number = iota[:, 0:E3].unsqueeze(1).broadcast_to([P, NB2, E3])
            dve.wait_ge(lg_done, NB2)
            link(dve.tensor_copy(lg[:, :, :].rearrange(f3), ps_lg[:, 0:NB2 * E3]))
            link(dve.tensor_reduce(red[:, 0, :], lg[:, :, :], AX.X, ALU.max))
            dve.tensor_tensor(t8[:, :, :], lg[:, :, :], wide(red[:, 0, :]), ALU.subtract).then_inc(lg_ready, 1)
            link(dve.tensor_scalar(real[:, :], tokv2[:, :], 0.0, None, ALU.is_gt))
            dve.wait_ge(exp_done, 1)
            link(dve.tensor_reduce(red[:, 1, :], pr[:, :, :], AX.X, ALU.add))
            link(dve.reciprocal(red[:, 2, :], red[:, 1, :]))
            link(dve.tensor_tensor(pr[:, :, :], pr[:, :, :], wide(red[:, 2, :]), ALU.mult))

            def largest(mask, score):
                link(dve.tensor_reduce(score, pr[:, :, :], AX.X, ALU.max))
                link(dve.tensor_tensor(t8[:, :, :], pr[:, :, :], wide(score), ALU.is_lt))
                link(dve.scalar_tensor_tensor(t8[:, :, :].rearrange(f3), t8[:, :, :].rearrange(f3), float(E3),
                                              lg[:, :, :].rearrange(f3), ALU.mult, ALU.add))
                link(dve.tensor_reduce(red[:, 3, :], t8[:, :, :], AX.X, ALU.min))
                link(dve.tensor_tensor(mask, lg[:, :, :], wide(red[:, 3, :]), ALU.is_equal))

            link(dve.tensor_copy(lg[:, :, :], number))
            largest(m1[:, :, :], red[:, 4, :])
            link(dve.scalar_tensor_tensor(pr[:, :, :].rearrange(f3), m1[:, :, :].rearrange(f3), -2.0,
                                          pr[:, :, :].rearrange(f3), ALU.mult, ALU.add))
            largest(m2[:, :, :], red[:, 5, :])
            link(dve.tensor_tensor(m1[:, :, :], m1[:, :, :], wide(real[:, :]), ALU.mult))
            link(dve.tensor_tensor(m2[:, :, :], m2[:, :, :], wide(real[:, :]), ALU.mult))
            dve.tensor_tensor(mb[:, :, :], m1[:, :, :], m2[:, :, :], ALU.add).then_inc(mask3_done, 1)
            link(dve.tensor_tensor(red[:, 6, :], red[:, 4, :], red[:, 5, :], ALU.add))
            link(dve.reciprocal(red[:, 6, :], red[:, 6, :]))
            alphas = alpha_b[:, :].unsqueeze(1).broadcast_to([P, NB2, E3])
            for k, m in ((0, m1), (1, m2)):
                link(dve.tensor_tensor(red[:, 4 + k, :], red[:, 4 + k, :], red[:, 6, :], ALU.mult))
                link(dve.tensor_tensor(t8[:, :, :], m[:, :, :], alphas, ALU.mult))
                link(dve.tensor_reduce(red[:, 7, :], t8[:, :, :], AX.X, ALU.add))
                link(dve.tensor_tensor(red[:, 4 + k, :], red[:, 4 + k, :], red[:, 7, :], ALU.mult))
            dve.wait_ge(rank3_done, 1)
            place(E3, NB2, tot3, cum3, rank3, NB3, eb3, eb3_done)
            for k, m in ((0, m1), (1, m2)):
                link(dve.tensor_tensor(t8[:, :, :], rank3[:, :, :], m[:, :, :], ALU.mult))
                link(dve.tensor_reduce(slot3[:, 0, k, :], t8[:, :, :], AX.X, ALU.add))
            link(dve.tensor_copy(slot3_i[:, 0, :, :], slot3[:, 0, :, :]))
            link(dve.tensor_scalar(slot3_i[:, 1, :, :], slot3_i[:, 0, :, :], P - 1, None, ALU.bitwise_and))
            link(dve.tensor_scalar(slot3_i[:, 2, :, :], slot3_i[:, 0, :, :], 7, None, ALU.arith_shift_right))
            link(dve.tensor_copy(slot3[:, :, :, :], slot3_i[:, 1:3, :, :]))
            for k in range(TOPK):
                for t in range(NB2):
                    n = NB2 * k + t
                    wait(dve, hot3_used, n - 3)
                    dve.tensor_scalar(onehot3[:, n % 4, :], iota[:, :], slot3[:, 0, k, t:t + 1], None, ALU.is_equal)
                    dve.tensor_scalar(onehotb3[:, n % 4, 0, :], iota[:, 0:NB3], slot3[:, 1, k, t:t + 1],
                                      tokv2[:, t:t + 1], ALU.is_equal, ALU.mult)
                    dve.tensor_scalar(onehotb3[:, n % 4, 1, :], iota[:, 0:NB3], slot3[:, 1, k, t:t + 1],
                                      red[:, 4 + k, t:t + 1], ALU.is_equal, ALU.mult).then_inc(hot3, 1)
            dve.wait_ge(hot3_used, TOPK * NB2)
            rows_of(ps_route[:, 0:NB3], row3[:, 0:NB3], eb_f, NB3).then_inc(row3_done, 1)
            dve.tensor_copy(w3[:, :], ps_route[:, NB3:2 * NB3]).then_inc(w3_done, 1)
            dve.wait_ge(w3_done, 1)

            for m in range(12, 2 * E3):
                low_weights(m)

            def expert_of(j):
                dve.wait_ge(eb3_done, 1)
                return dve.value_load(eb3[0:1, ds(j, 1)], min_val=0, max_val=E3 - 1)

            def low_x3(j):
                dve.wait_ge(xgT_hi, j + 1)
                dve.scalar_tensor_tensor(xgT[:, 1, :], ps_xt[:, :], X_SCALE, xgT[:, 0, :],
                                         ALU.mult, ALU.subtract).then_inc(xgT_lo, 1)

            def step3(j, k):
                static = isinstance(j, int)
                k1 = (k - 1) % 2
                if not static or j < NB3:
                    exp_in = expert_of(j)
                    dve.wait_ge(z3_done, j + 1)
                    wait(dve, hg_done, j)
                    if static and j == 0:
                        dve.wait_ge(bias_in, 32)
                    dve.scalar_tensor_tensor(hb[:, :], ps_h[:, :], undo[:, 0:1], one(bias1[:, ds(exp_in, 1), :]),
                                             ALU.mult, ALU.add).then_inc(hb_done, 1)
                if not static or j + 1 < NB3:
                    low_x3(j + 1)
                if not static or j >= 1:
                    exp_out = expert_of(j - 1)
                    dve.wait_ge(y3_done, j)
                    wait(dve, added, 16 * (j - 2) if not static or j > 2 else 0)
                    dve.scalar_tensor_tensor(yb[:, k1, :], ps_o[:, :], undo[:, 1:2], one(bias2[:, ds(exp_out, 1), :]),
                                             ALU.mult, ALU.add).then_inc(yb_done, 1)
                    dve.wait_ge(yb_done, j)
                    dve.tensor_scalar(yb[:, k1, :], yb[:, k1, :], w3[:, ds(j - 1, 1)], None, ALU.mult).then_inc(yw_done, 1)
                if not static or j < NB3:
                    dve.wait_ge(hgT_hi, j + 1)
                    dve.scalar_tensor_tensor(hgT[:, 1, :], ps_ht[:, :], h_scale, hgT[:, 0, :],
                                             ALU.mult, ALU.subtract).then_inc(hgT_lo, 1)

            low_x3(0)
            for j in range(4):
                step3(j, j)
            with dve.Fori(4, 36, 4) as j:
                for k in range(4):
                    step3(j + k, k)
            for j in range(36, NB3 + 1):
                step3(j, j % 4)


_INS = ["x", "tid", "ctxT", "wiT", "wfT", "wgT", "gnorm", "woT", "gate_w", "expert_w", "fc1_b", "fc2_b", "alpha"]


def kernel(**inputs):
    import numpy as np
    import concourse.bacc as bacc
    from concourse.bass_utils import run_bass_kernel_spmd

    given = {k: np.asarray(v) for k, v in inputs.items()}
    laid = {
        "x": given["x"].reshape(TOK, D),
        "tid": given["itok_BxS_13_99985"].reshape(T16, P).T,
        "ctxT": given["ctx_2048"].transpose(0, 2, 1).reshape(E2 * D, D),
        "wiT": given["L0_attn_Wi"].T, "wfT": given["L0_attn_Wf"].T, "wgT": given["L0_attn_Wg"].T,
        "gnorm": given["L0_attn_g_norm_weight"].reshape(C, P).T, "woT": given["L0_attn_Wo"].T,
        "gate_w": given["L0_ffn_gate_w"],
        "expert_w": np.concatenate([given["L0_ffn_fc1_w"], given["L0_ffn_fc2_w"]]).reshape(2 * E3 * D, D),
        "fc1_b": given["L0_ffn_fc1_b"], "fc2_b": given["L0_ffn_fc2_b"], "alpha": given["L0_ffn_alpha"],
    }
    nc = bacc.Bacc("TRN2", target_bir_lowering=False, num_devices=1)
    arrays, args = {}, []
    for name in _INS:
        a = np.ascontiguousarray(laid[name])
        arrays[f"in_{name}"] = a
        args.append(nc.dram_tensor(f"in_{name}", a.shape, mybir.dt.from_np(a.dtype), kind="ExternalInput").ap())
    out = nc.dram_tensor("out_rows", (ROWS, D), mybir.dt.float32, kind="ExternalOutput").ap()
    decoder_layer(nc, *args, out)
    r = run_bass_kernel_spmd(nc, [arrays], core_ids=[0])
    return r.results[0]["out_rows"][:TOK].reshape(BATCH, SEQ, D)
```
